# Optimizing a Trainium2 kernel written in Bass

```python
import numpy as np
import jax
import jax.numpy as jnp

def _softmax(x, axis=-1):
    return jax.nn.softmax(x, axis=axis)

def _gelu(x):
    return jax.nn.gelu(x, approximate=True)

def _silu(x):
    return jax.nn.silu(x)

def _sigmoid(x):
    return jax.nn.sigmoid(x)

def _layernorm(x, axis=-1, eps=1e-05):
    m = jnp.mean(x, axis=axis, keepdims=True)
    v = jnp.var(x, axis=axis, keepdims=True)
    return (x - m) / jnp.sqrt(v + eps)

def _scatter_add(tgt, idx, src, axis=0):
    return tgt.at[idx].add(src)

def _segment_sum(src, seg, n):
    return jax.ops.segment_sum(src, seg, n)
kernel_name = 'mk_dlrm_tower_d1_rec_r8_a27859'

def setup_inputs(seed: int=0):
    np.random.seed(seed)
    _w = jnp.asarray

    def _rec_inputs():
        import jax
        import jax.numpy as jnp
        _tk = jax.random.key(seed)
        dense_ctx = jax.random.normal(jax.random.fold_in(_tk, 190), (512, 16), jnp.float32)
        ids = jnp.stack([jax.random.randint(jax.random.fold_in(_tk, 200 + f), (512,), 0, v, jnp.int32) for f, v in enumerate([1000, 1250, 1250, 1250, 1000, 1250, 125000, 12500, 1250, 1000, 12500, 1250, 1000, 1000, 1250, 1250, 1000, 1250, 1250, 1250, 1250, 1000, 1250, 125000, 12500, 125000, 1250, 1000, 1250, 1250, 1250, 1250])], axis=1)
        tbl_0 = 0.05 * jax.random.normal(jax.random.fold_in(_tk, 500 + 0), (1000, 64), jnp.float32)
        tbl_1 = 0.05 * jax.random.normal(jax.random.fold_in(_tk, 500 + 1), (1250, 64), jnp.float32)
        tbl_2 = 0.05 * jax.random.normal(jax.random.fold_in(_tk, 500 + 2), (1250, 64), jnp.float32)
        tbl_3 = 0.05 * jax.random.normal(jax.random.fold_in(_tk, 500 + 3), (1250, 64), jnp.float32)
        tbl_4 = 0.05 * jax.random.normal(jax.random.fold_in(_tk, 500 + 4), (1000, 64), jnp.float32)
        tbl_5 = 0.05 * jax.random.normal(jax.random.fold_in(_tk, 500 + 5), (1250, 64), jnp.float32)
        tbl_6 = 0.05 * jax.random.normal(jax.random.fold_in(_tk, 500 + 6), (125000, 64), jnp.float32)
        tbl_7 = 0.05 * jax.random.normal(jax.random.fold_in(_tk, 500 + 7), (12500, 64), jnp.float32)
        tbl_8 = 0.05 * jax.random.normal(jax.random.fold_in(_tk, 500 + 8), (1250, 64), jnp.float32)
        tbl_9 = 0.05 * jax.random.normal(jax.random.fold_in(_tk, 500 + 9), (1000, 64), jnp.float32)
        tbl_10 = 0.05 * jax.random.normal(jax.random.fold_in(_tk, 500 + 10), (12500, 64), jnp.float32)
        tbl_11 = 0.05 * jax.random.normal(jax.random.fold_in(_tk, 500 + 11), (1250, 64), jnp.float32)
        tbl_12 = 0.05 * jax.random.normal(jax.random.fold_in(_tk, 500 + 12), (1000, 64), jnp.float32)
        tbl_13 = 0.05 * jax.random.normal(jax.random.fold_in(_tk, 500 + 13), (1000, 64), jnp.float32)
        tbl_14 = 0.05 * jax.random.normal(jax.random.fold_in(_tk, 500 + 14), (1250, 64), jnp.float32)
        tbl_15 = 0.05 * jax.random.normal(jax.random.fold_in(_tk, 500 + 15), (1250, 64), jnp.float32)
        tbl_16 = 0.05 * jax.random.normal(jax.random.fold_in(_tk, 500 + 16), (1000, 64), jnp.float32)
        tbl_17 = 0.05 * jax.random.normal(jax.random.fold_in(_tk, 500 + 17), (1250, 64), jnp.float32)
        tbl_18 = 0.05 * jax.random.normal(jax.random.fold_in(_tk, 500 + 18), (1250, 64), jnp.float32)
        tbl_19 = 0.05 * jax.random.normal(jax.random.fold_in(_tk, 500 + 19), (1250, 64), jnp.float32)
        tbl_20 = 0.05 * jax.random.normal(jax.random.fold_in(_tk, 500 + 20), (1250, 64), jnp.float32)
        tbl_21 = 0.05 * jax.random.normal(jax.random.fold_in(_tk, 500 + 21), (1000, 64), jnp.float32)
        tbl_22 = 0.05 * jax.random.normal(jax.random.fold_in(_tk, 500 + 22), (1250, 64), jnp.float32)
        tbl_23 = 0.05 * jax.random.normal(jax.random.fold_in(_tk, 500 + 23), (125000, 64), jnp.float32)
        tbl_24 = 0.05 * jax.random.normal(jax.random.fold_in(_tk, 500 + 24), (12500, 64), jnp.float32)
        tbl_25 = 0.05 * jax.random.normal(jax.random.fold_in(_tk, 500 + 25), (125000, 64), jnp.float32)
        tbl_26 = 0.05 * jax.random.normal(jax.random.fold_in(_tk, 500 + 26), (1250, 64), jnp.float32)
        tbl_27 = 0.05 * jax.random.normal(jax.random.fold_in(_tk, 500 + 27), (1000, 64), jnp.float32)
        tbl_28 = 0.05 * jax.random.normal(jax.random.fold_in(_tk, 500 + 28), (1250, 64), jnp.float32)
        tbl_29 = 0.05 * jax.random.normal(jax.random.fold_in(_tk, 500 + 29), (1250, 64), jnp.float32)
        tbl_30 = 0.05 * jax.random.normal(jax.random.fold_in(_tk, 500 + 30), (1250, 64), jnp.float32)
        tbl_31 = 0.05 * jax.random.normal(jax.random.fold_in(_tk, 500 + 31), (1250, 64), jnp.float32)
        _rk = jax.random.fold_in(_tk, 7)
        W_top1 = 0.0441942 * jax.random.normal(jax.random.fold_in(_tk, 801), (512, 512), jnp.float32)
        W_top2 = 0.0441942 * jax.random.normal(jax.random.fold_in(_tk, 802), (512, 256), jnp.float32)
        W_top3 = 0.0625 * jax.random.normal(jax.random.fold_in(_tk, 803), (256, 1), jnp.float32)
        b_top1 = jnp.zeros((512,), jnp.float32)
        b_top2 = jnp.zeros((256,), jnp.float32)
        return (dense_ctx, ids, tbl_0, tbl_1, tbl_2, tbl_3, tbl_4, tbl_5, tbl_6, tbl_7, tbl_8, tbl_9, tbl_10, tbl_11, tbl_12, tbl_13, tbl_14, tbl_15, tbl_16, tbl_17, tbl_18, tbl_19, tbl_20, tbl_21, tbl_22, tbl_23, tbl_24, tbl_25, tbl_26, tbl_27, tbl_28, tbl_29, tbl_30, tbl_31, W_top1, b_top1, W_top2, b_top2, W_top3)
    dense_ctx, ids, tbl_0, tbl_1, tbl_2, tbl_3, tbl_4, tbl_5, tbl_6, tbl_7, tbl_8, tbl_9, tbl_10, tbl_11, tbl_12, tbl_13, tbl_14, tbl_15, tbl_16, tbl_17, tbl_18, tbl_19, tbl_20, tbl_21, tbl_22, tbl_23, tbl_24, tbl_25, tbl_26, tbl_27, tbl_28, tbl_29, tbl_30, tbl_31, W_top1, b_top1, W_top2, b_top2, W_top3 = _rec_inputs()

    def _L0_rec_setup():
        import jax, jax.numpy as jnp
        import numpy as np
        B, F, E = (512, 32, 64)
        P = F * (F - 1) // 2
        key = jax.random.key(seed)
        k1, k2 = jax.random.split(key)
        x = jax.random.normal(k1, (B, F, E), dtype=jnp.float32)
        kernel = jax.random.normal(k2, (E, P, E), dtype=jnp.float32) * 0.05
        return {'x': x, 'kernel': kernel}
    _L0_rec_all = _L0_rec_setup()
    _L0_rec_in = {k: v for k, v in _L0_rec_all.items() if k in ('kernel',)}
    del _L0_rec_all
    return {'dense_ctx': dense_ctx, 'ids': ids, 'tbl_0': tbl_0, 'tbl_1': tbl_1, 'tbl_2': tbl_2, 'tbl_3': tbl_3, 'tbl_4': tbl_4, 'tbl_5': tbl_5, 'tbl_6': tbl_6, 'tbl_7': tbl_7, 'tbl_8': tbl_8, 'tbl_9': tbl_9, 'tbl_10': tbl_10, 'tbl_11': tbl_11, 'tbl_12': tbl_12, 'tbl_13': tbl_13, 'tbl_14': tbl_14, 'tbl_15': tbl_15, 'tbl_16': tbl_16, 'tbl_17': tbl_17, 'tbl_18': tbl_18, 'tbl_19': tbl_19, 'tbl_20': tbl_20, 'tbl_21': tbl_21, 'tbl_22': tbl_22, 'tbl_23': tbl_23, 'tbl_24': tbl_24, 'tbl_25': tbl_25, 'tbl_26': tbl_26, 'tbl_27': tbl_27, 'tbl_28': tbl_28, 'tbl_29': tbl_29, 'tbl_30': tbl_30, 'tbl_31': tbl_31, 'W_top1': W_top1, 'b_top1': b_top1, 'W_top2': W_top2, 'b_top2': b_top2, 'W_top3': W_top3, 'L0_rec_kernel': _L0_rec_in['kernel']}

def reference(dense_ctx, ids, tbl_0, tbl_1, tbl_2, tbl_3, tbl_4, tbl_5, tbl_6, tbl_7, tbl_8, tbl_9, tbl_10, tbl_11, tbl_12, tbl_13, tbl_14, tbl_15, tbl_16, tbl_17, tbl_18, tbl_19, tbl_20, tbl_21, tbl_22, tbl_23, tbl_24, tbl_25, tbl_26, tbl_27, tbl_28, tbl_29, tbl_30, tbl_31, W_top1, b_top1, W_top2, b_top2, W_top3, L0_rec_kernel):
    import jax
    import jax.numpy as jnp

    def _L0_rec_ref(x, kernel):
        import jax, jax.numpy as jnp
        import numpy as np
        B, F, E = (512, 32, 64)
        P = F * (F - 1) // 2
        nf = x.shape[1]
        row_idx, col_idx = np.triu_indices(nf, k=1)
        p = x[:, row_idx, :]
        q = x[:, col_idx, :]
        kp = jnp.einsum('bpe,fpe,bpf->bp', p, kernel, q)
        return kp
    e = jnp.stack([tbl_0[ids[:, 0]], tbl_1[ids[:, 1]], tbl_2[ids[:, 2]], tbl_3[ids[:, 3]], tbl_4[ids[:, 4]], tbl_5[ids[:, 5]], tbl_6[ids[:, 6]], tbl_7[ids[:, 7]], tbl_8[ids[:, 8]], tbl_9[ids[:, 9]], tbl_10[ids[:, 10]], tbl_11[ids[:, 11]], tbl_12[ids[:, 12]], tbl_13[ids[:, 13]], tbl_14[ids[:, 14]], tbl_15[ids[:, 15]], tbl_16[ids[:, 16]], tbl_17[ids[:, 17]], tbl_18[ids[:, 18]], tbl_19[ids[:, 19]], tbl_20[ids[:, 20]], tbl_21[ids[:, 21]], tbl_22[ids[:, 22]], tbl_23[ids[:, 23]], tbl_24[ids[:, 24]], tbl_25[ids[:, 25]], tbl_26[ids[:, 26]], tbl_27[ids[:, 27]], tbl_28[ids[:, 28]], tbl_29[ids[:, 29]], tbl_30[ids[:, 30]], tbl_31[ids[:, 31]]], axis=1)
    z = _L0_rec_ref(e, L0_rec_kernel)
    z = z.reshape(z.shape[0], -1)
    h = jnp.concatenate([z, dense_ctx], axis=1)
    h = jnp.maximum(h @ W_top1 + b_top1, 0.0)
    h = jnp.maximum(h @ W_top2 + b_top2, 0.0)
    y = h @ W_top3
    return y

_drawn_inputs = setup_inputs


def setup_inputs(seed=0):
    import zlib

    import numpy as np

    out = dict(_drawn_inputs(seed))
    spreads = {'b_top1': (0.0, 0.1), 'b_top2': (0.0, 0.1)}
    factors = {'tbl_0': 6.621,
     'tbl_1': 5.984,
     'tbl_2': 5.666,
     'tbl_3': 5.746,
     'tbl_4': 5.085,
     'tbl_5': 6.194,
     'tbl_6': 5.668,
     'tbl_7': 4.962,
     'tbl_8': 5.825,
     'tbl_9': 5.568,
     'tbl_10': 5.702,
     'tbl_11': 5.384,
     'tbl_12': 5.096,
     'tbl_13': 5.002,
     'tbl_14': 6.23,
     'tbl_15': 5.716,
     'tbl_16': 5.421,
     'tbl_17': 6.147,
     'tbl_18': 5.273,
     'tbl_19': 5.546,
     'tbl_20': 5.244,
     'tbl_21': 5.804,
     'tbl_22': 6.65,
     'tbl_23': 6.156,
     'tbl_24': 5.846,
     'tbl_25': 5.357,
     'tbl_26': 5.784,
     'tbl_27': 5.93,
     'tbl_28': 5.909,
     'tbl_29': 5.748,
     'tbl_30': 6.124,
     'tbl_31': 6.46}
    for name, (base, spread) in spreads.items():
        noise = np.random.default_rng([zlib.crc32(name.encode()), seed]).standard_normal(out[name].shape)
        drawn = base * np.exp(spread * noise) if base else spread * noise
        out[name] = jnp.asarray(drawn.astype(out[name].dtype))
    for name, factor in factors.items():
        out[name] = (out[name] * factor).astype(out[name].dtype)
    return out
```

```python
from contextlib import ExitStack

import numpy as np

import concourse.bass as bass
from concourse import mybir

ALU = mybir.AluOpType
ACT = mybir.ActivationFunctionType
F32 = mybir.dt.float32
F32R = mybir.dt.float32r
I32 = mybir.dt.int32

B, F, E = 512, 32, 64
D1, D2, DENSE = 512, 256, 16
P = 128
BT = B // P
NC = F // 2
NPAIR = F * (F - 1) // 2
ZT = (NPAIR + DENSE) // P

CHUNK_UNITS = 4
CHUNK_BLOCKS = 2 * CHUNK_UNITS
CHUNK = CHUNK_BLOCKS * P
K_SLOTS = 3
T_SLOTS = 3
PROD_SLOTS = 4
SPLIT_SLOTS = 2
X_SLOTS = 6
SEL_AT = 31


def pair_index(i, j):
    return i * (2 * F - i - 1) // 2 + j - i - 1


def make_units():
    units = []
    for c in range(NC):
        for a in range(c):
            units.append(dict(by=(a, a), over=(2 * c, 2 * c + 1), last=c, lone=False))
        if c % 2:
            units.append(dict(by=(c - 1, c), over=(2 * c - 1, 2 * c + 1), last=c, lone=True))
    return units


def block_pairs(unit, q):
    i, j = 2 * unit["by"][q], unit["over"][q]
    return [(i, j)] if unit["lone"] else [(i, j), (i + 1, j)]


def place_rows(units):
    room = [[32] * 4 for _ in range(ZT)]
    room[ZT - 1][3] -= DENSE
    tile, places, rows = 0, [], np.full(NPAIR + DENSE, -1, np.int64)
    for unit in units:
        quads = []
        for q in range(2):
            size = len(block_pairs(unit, q))
            if not any(room[tile]):
                tile += 1
            quad = quads[0] if unit["lone"] and q else int(np.argmax(room[tile]))
            quads.append(quad)
            full = 32 - (DENSE if (tile, quad) == (ZT - 1, 3) else 0)
            at = full - room[tile][quad]
            room[tile][quad] -= size
            assert room[tile][quad] >= 0
            for k, (i, j) in enumerate(block_pairs(unit, q)):
                rows[tile * P + 32 * quad + at + k] = pair_index(i, j)
            places.append((tile, quad, at, at == 0, room[tile][quad] == 0))
    rows[rows < 0] = NPAIR + np.arange(DENSE)
    return places, rows


UNITS = make_units()
PLACES, Z_ROWS = place_rows(UNITS)
NU = len(UNITS)
N_CHUNKS = NU // CHUNK_UNITS
Z_CLOSES = [max(n for n, p in enumerate(PLACES) if p[0] == t) for t in range(ZT)]
Z_SIGNALS = sorted(set(Z_CLOSES) | set(range(3, 2 * NU, 4)))


def z_signal(block):
    return 1 + sum(n < block for n in Z_SIGNALS)


ONE_ROW_END = P - DENSE

GATHER, FIRST_GATHER, UNIT, JOB, EVACUATE, SPLIT = 8.5, 7.0, 1.4, 0.45, 1.3, 1.6
POOL_FROM = GATHER * NC + FIRST_GATHER


def make_steps():
    steps, at = [("ksplit", m) for m in range(K_SLOTS - 1)], 0.0
    arrived = [FIRST_GATHER + GATHER * (c + 1) for c in range(NC)]
    jobs = [(arrived[c] + (SPLIT if k else 0), c, k) for c in range(NC) for k in range(3)]
    ready_at = [None] * NC
    split, job, unit, last_job, on_pool = 0, 0, 0, -9.0, []
    while unit < NU:
        if split < NC and at >= arrived[split]:
            steps.append(("split", split))
            split += 1
        if job < len(jobs) and jobs[job][1] < split and at >= max(jobs[job][0], last_job + EVACUATE):
            steps.append(("job", job))
            last_job, at = at, at + JOB
            ready_at[jobs[job][1]] = at + EVACUATE
            job += 1
        elif job >= 3 * (UNITS[unit]["last"] + 1) and at >= ready_at[UNITS[unit]["last"]]:
            if unit % CHUNK_UNITS == 0 and unit // CHUNK_UNITS + K_SLOTS - 1 < N_CHUNKS:
                m = unit // CHUNK_UNITS + K_SLOTS - 1
                steps.append(("ksplit", m))
                if at > POOL_FROM:
                    on_pool.append(m)
            steps.append(("unit", unit))
            at += UNIT
            unit += 1
        else:
            at += 0.1
    return steps, on_pool


STEPS, POOL_CHUNKS = make_steps()
POOL_FIRST = POOL_CHUNKS[0]


def selectors():
    s = np.zeros((P, 2, 64), np.float32)
    s[:E, :, SEL_AT] = 1
    s[E:, 0, SEL_AT + 1] = 1
    return s


def build(nc, ids, tables, kblocks, dense_t, w1, b1, w2, b2, w3, ident, sel, y):
    with ExitStack() as ctx:
        def sb(name, shape, dt=F32):
            return ctx.enter_context(nc.sbuf_tensor(name, shape, dt))

        def sem(name):
            return ctx.enter_context(nc.semaphore(name))

        ids_sb = sb("ids_sb", [P, F, BT], I32)
        ident_sb = sb("ident_sb", [P, P])
        sel_sb = sb("sel_sb", [P, 2, 64])
        x_nat = sb("x_nat", [P, X_SLOTS, BT, 2, E])
        x_parts = sb("x_parts", [P, SPLIT_SLOTS, BT, 2, 2, E], F32R)
        x_t = sb("x_t", [P, NC, B])
        x_hl = sb("x_hl", [P, F, B], F32R)
        k_raw = sb("k_raw", [P, K_SLOTS, CHUNK])
        k_hi = sb("k_hi", [P, K_SLOTS, CHUNK], F32R)
        k_lo = sb("k_lo", [P, K_SLOTS, CHUNK], F32R)
        prod = sb("prod", [P, PROD_SLOTS, 2, B])
        z_t = sb("z_t", [P, ZT, B])
        w1_sb = sb("w1_sb", [P, ZT, D1])
        w2_sb = sb("w2_sb", [P, D1 // P, D2])
        w3_sb = sb("w3_sb", [P, D2 // P])
        b1_sb = sb("b1_sb", [P, D1 // P])
        b2_sb = sb("b2_sb", [P, D2 // P])
        h1_t = k_raw[:, 0:2, :].rearrange("p s (n b) -> p (s n) b", b=B)
        h2_t = k_raw[:, 2, :].rearrange("p (n b) -> p n b", b=B)
        y_sb = sb("y_sb", [1, B])

        t_ps = ctx.enter_context(nc.psum_tensor("t_ps", [P, 2 * T_SLOTS, B], F32))
        z_ps = ctx.enter_context(nc.psum_tensor("z_ps", [P, B], F32))
        turn_ps = ctx.enter_context(nc.psum_tensor("turn_ps", [P, BT, P], F32))

        ids_in = sem("ids_in")
        consts_in = sem("consts_in")
        tower_in = sem("tower_in")
        dense_in = sem("dense_in")
        gathered = [sem(f"gathered{c}") for c in range(NC)]
        k_in = [sem(f"k_in{s}") for s in range(K_SLOTS)]
        x_hi_done = sem("x_hi_done")
        x_lo_done = sem("x_lo_done")
        turned = sem("turned")
        turned_out = sem("turned_out")
        k_hi_done = sem("k_hi_done")
        k_lo_dve = sem("k_lo_dve")
        k_lo_pool = sem("k_lo_pool")
        t_done = sem("t_done")
        prod_done = sem("prod_done")
        z_summed = sem("z_summed")
        z_out = sem("z_out")
        h1_ps_done = sem("h1_ps_done")
        h1_act = sem("h1_act")
        h1_dve = sem("h1_dve")
        h2_ps_done = sem("h2_ps_done")
        h2_act = sem("h2_act")
        h2_dve = sem("h2_dve")
        bias_dve = sem("bias_dve")
        y_ps_done = sem("y_ps_done")
        y_done = sem("y_done")
        y_stored = sem("y_stored")

        block = ctx.enter_context(nc.Block())

        def wait_k_lo(eng, m):
            if m < POOL_FIRST:
                eng.wait_ge(k_lo_dve, m + 1)
            else:
                eng.wait_ge(k_lo_pool, m - POOL_FIRST + 1)

        @block.sync
        def _(sp):
            sp.dma_start(ids_sb[:, :, :], ids).then_inc(ids_in, 16)
            sp.dma_start(ident_sb[:, :], ident).then_inc(consts_in, 16)
            sp.dma_start(sel_sb[:, :, :], sel).then_inc(consts_in, 16)
            for m in range(N_CHUNKS):
                s = m % K_SLOTS
                if m >= K_SLOTS:
                    wait_k_lo(sp, m - K_SLOTS)
                for half in range(2):
                    sp.dma_start(k_raw[half * E:(half + 1) * E, s, :],
                                 kblocks[:, m * CHUNK:(m + 1) * CHUNK]).then_inc(k_in[s], 16)
                if m == K_SLOTS - 1:
                    sp.dma_start(w1_sb[:, :, :], w1).then_inc(tower_in, 16)
                    sp.dma_start(w2_sb[:, :, :], w2).then_inc(tower_in, 16)
                    sp.dma_start(w3_sb[:, :], w3).then_inc(tower_in, 16)
                    sp.dma_start(b1_sb[:, :], b1).then_inc(tower_in, 16)
                    sp.dma_start(b2_sb[:, :], b2).then_inc(tower_in, 16)
                    sp.dma_start(z_t[P - DENSE:P, ZT - 1, :], dense_t).then_inc(dense_in, 16)
            sp.wait_ge(y_done, 1)
            sp.dma_start(y, y_sb[:, :]).then_inc(y_stored, 16)
            sp.wait_ge(y_stored, 16)

        @block.gpsimd
        def _(pool):
            pool.wait_ge(ids_in, 16)
            for f in range(F):
                c = f // 2
                if f % 2 == 0 and c >= X_SLOTS:
                    pool.wait_ge(x_lo_done, c - X_SLOTS + 1)
                    pool.wait_ge(turned, 3 * (c - X_SLOTS) + 1)
                for bt in range(BT):
                    pool.indirect_dma_start(
                        x_nat[:, c % X_SLOTS, bt, f % 2, :], None, tables[f],
                        bass.IndirectOffsetOnAxis(ap=ids_sb[:, f, bt:bt + 1], axis=0),
                    ).then_inc(gathered[c], 16)
            for m in range(POOL_FIRST, N_CHUNKS):
                s = m % K_SLOTS
                pool.wait_ge(k_hi_done, m + 1)
                pool.wait_ge(t_done, CHUNK_UNITS * (m - K_SLOTS + 1))
                nc.gpsimd.tensor_tensor(k_lo[:, s, :], k_raw[:, s, :], k_hi[:, s, :].bitcast(F32),
                                        ALU.subtract).then_inc(k_lo_pool, 1)

        @block.scalar
        def _(act):
            def finish_z(batch):
                for t in range(ZT):
                    if 4 * (batch - 1) <= Z_CLOSES[t] < 4 * batch:
                        act.wait_ge(z_summed, z_signal(Z_CLOSES[t]))
                        rows = ONE_ROW_END if t == ZT - 1 else P
                        nc.scalar.activation(z_t[0:rows, t, :], z_ps[0:rows, :], ACT.Copy).then_inc(z_out, 1)

            batch = 0
            for what, n in STEPS:
                if what == "ksplit":
                    s = n % K_SLOTS
                    act.wait_ge(k_in[s], 32 * (n // K_SLOTS + 1))
                    if n >= K_SLOTS:
                        act.wait_ge(t_done, CHUNK_UNITS * (n - K_SLOTS + 1))
                    nc.scalar.activation(k_hi[:, s, :], k_raw[:, s, :], ACT.Copy).then_inc(k_hi_done, 1)
                if what == "split":
                    act.wait_ge(gathered[n], 16 * 2 * BT)
                    if n >= SPLIT_SLOTS:
                        act.wait_ge(turned, 3 * (n - SPLIT_SLOTS + 1))
                    nc.scalar.activation(x_parts[:, n % SPLIT_SLOTS, :, :, 0, :], x_nat[:, n % X_SLOTS, :, :, :],
                                         ACT.Copy).then_inc(x_hi_done, 1)
                if what == "job":
                    c, k = divmod(n, 3)
                    act.wait_ge(turned, n + 1)
                    out = x_t[:, c, :] if k == 0 else x_hl[:, 2 * c + k - 1, :]
                    nc.scalar.activation(out, turn_ps[:, :, :].rearrange("p t b -> p (t b)"),
                                         ACT.Copy).then_inc(turned_out, 1)
                if what == "unit" and n % 2 and n > 1:
                    batch += 1
                    finish_z(batch)

            finish_z(batch + 1)
            for n in range(0, D1 // P, 2):
                act.wait_ge(h1_ps_done, n + 1)
                act.wait_ge(tower_in, 16 * 5)
                nc.scalar.activation(h1_t[:, n, :], t_ps[:, n, :], ACT.Relu,
                                     bias=b1_sb[:, n:n + 1]).then_inc(h1_act, 1)
            act.wait_ge(h2_ps_done, 1)
            nc.scalar.activation(h2_t[:, 0, :], t_ps[:, 4, :], ACT.Relu,
                                 bias=b2_sb[:, 0:1]).then_inc(h2_act, 1)
            act.wait_ge(y_ps_done, 1)
            nc.scalar.activation(y_sb[:, :], z_ps[0:1, :], ACT.Copy).then_inc(y_done, 1)

        @block.vector
        def _(dve):
            for what, n in STEPS:
                if what == "split":
                    dve.wait_ge(x_hi_done, n + 1)
                    parts = x_parts[:, n % SPLIT_SLOTS, :, :, :, :]
                    nc.vector.tensor_tensor(parts[:, :, :, 1, :], x_nat[:, n % X_SLOTS, :, :, :],
                                            parts[:, :, :, 0, :].bitcast(F32),
                                            ALU.subtract).then_inc(x_lo_done, 1)
                if what == "ksplit" and n < POOL_FIRST:
                    s = n % K_SLOTS
                    dve.wait_ge(k_hi_done, n + 1)
                    if n >= K_SLOTS:
                        dve.wait_ge(t_done, CHUNK_UNITS * (n - K_SLOTS + 1))
                    nc.vector.tensor_tensor(k_lo[:, s, :], k_raw[:, s, :], k_hi[:, s, :].bitcast(F32),
                                            ALU.subtract).then_inc(k_lo_dve, 1)
                if what == "unit":
                    unit, s = UNITS[n], n % T_SLOTS
                    a, a2 = unit["by"]
                    if a == a2:
                        by = x_t[:, a:a + 1, :].to_broadcast([P, 2, B])
                    else:
                        by = x_t[:, a:a2 + 1, :]
                    dve.wait_ge(t_done, n + 1)
                    dve.wait_ge(turned_out, 3 * a2 + 1)
                    if n >= PROD_SLOTS:
                        dve.wait_ge(z_summed, z_signal(2 * (n - PROD_SLOTS) + 1))
                    nc.vector.tensor_tensor(prod[:, n % PROD_SLOTS, :, :], t_ps[:, 2 * s:2 * s + 2, :],
                                            by, ALU.mult).then_inc(prod_done, 1)
            for k, n in enumerate(range(1, D1 // P, 2)):
                dve.wait_ge(h1_ps_done, n + 1)
                dve.wait_ge(tower_in, 16 * 5)
                nc.vector.tensor_scalar(h1_t[:, n, :], t_ps[:, n, :], b1_sb[:, n:n + 1], 0.0,
                                        ALU.add, ALU.max).then_inc(h1_dve, 1)
            dve.wait_ge(h2_ps_done, 2)
            nc.vector.tensor_scalar(h2_t[:, 1, :], t_ps[:, 5, :], b2_sb[:, 1:2], 0.0,
                                    ALU.add, ALU.max).then_inc(h2_dve, 1)

        @block.tensor
        def _(pe):
            def job(n):
                c, k = divmod(n, 3)
                if k == 0:
                    pe.wait_ge(gathered[c], 16 * 2 * BT)
                else:
                    pe.wait_ge(x_lo_done, c + 1)
                if n:
                    pe.wait_ge(turned_out, n)
                for bt in range(BT):
                    if k == 0:
                        src = x_nat[:, c % X_SLOTS, bt, :, :]
                    else:
                        src = x_parts[:, c % SPLIT_SLOTS, bt, k - 1, :, :].bitcast(F32)
                    last = nc.tensor.transpose(turn_ps[:, bt, :], src.rearrange("p a e -> p (a e)"),
                                               ident_sb[:, :])
                last.then_inc(turned, 1)

            def products(u):
                unit, s = UNITS[u], u % T_SLOTS
                m = u // CHUNK_UNITS
                if u % CHUNK_UNITS == 0:
                    wait_k_lo(pe, m)
                pe.wait_ge(turned_out, 3 * unit["last"] + 3)
                if u >= T_SLOTS:
                    pe.wait_ge(prod_done, u - T_SLOTS + 1)
                for q in range(2):
                    at = ((2 * u + q) % CHUNK_BLOCKS) * P
                    j = unit["over"][q]
                    for k, part in enumerate((k_hi, k_lo)):
                        last = nc.tensor.matmul(t_ps[:, 2 * s + q, :], part[:, m % K_SLOTS, at:at + P],
                                                x_hl[:, j, :], start=(k == 0), stop=(k == 1))
                last.then_inc(t_done, 1)

            def sums(batch):
                pe.wait_ge(prod_done, 2 * batch + 2)
                for n in range(4 * batch, 4 * batch + 4):
                    tile, quad, at, first, final = PLACES[n]
                    lone = int(UNITS[n // 2]["lone"])
                    if tile and n == Z_CLOSES[tile - 1] + 1:
                        pe.wait_ge(z_out, tile)
                    last = nc.tensor.matmul(z_ps[32 * quad:32 * quad + 32, :],
                                            sel_sb[:, lone, SEL_AT - at:SEL_AT - at + 32],
                                            prod[:, (n // 2) % PROD_SLOTS, n % 2, :],
                                            start=first, stop=final)
                    if n in Z_SIGNALS:
                        last.then_inc(z_summed, 1)

            def tower1(t):
                pe.wait_ge(z_out, t + 1)
                for n in range(D1 // P):
                    last = nc.tensor.matmul(t_ps[:, n, :], w1_sb[:, t, n * P:(n + 1) * P], z_t[:, t, :],
                                            start=(t == 0), stop=(t == ZT - 1))
                    if t == ZT - 1:
                        last.then_inc(h1_ps_done, 1)

            pe.wait_ge(consts_in, 32)
            for what, n in STEPS:
                if what == "job":
                    job(n)
                if what == "unit":
                    products(n)
                    if n % 2 and n > 1:
                        sums((n - 3) // 2)
            pe.wait_ge(tower_in, 16 * 5)
            pe.wait_ge(dense_in, 16)
            sums(NU // 2 - 1)
            for t in range(ZT):
                tower1(t)
            for t in range(D1 // P):
                if t % 2 == 0:
                    pe.wait_ge(h1_act, t // 2 + 1)
                else:
                    pe.wait_ge(h1_dve, t // 2 + 1)
                for n in range(D2 // P):
                    last = nc.tensor.matmul(t_ps[:, 4 + n, :], w2_sb[:, t, n * P:(n + 1) * P],
                                            h1_t[:, t, :], start=(t == 0), stop=(t == D1 // P - 1))
                    if t == D1 // P - 1:
                        last.then_inc(h2_ps_done, 1)
            pe.wait_ge(h2_act, 1)
            nc.tensor.matmul(z_ps[0:1, :], w3_sb[:, 0:1], h2_t[:, 0, :], start=True, stop=False)
            pe.wait_ge(h2_dve, 1)
            nc.tensor.matmul(z_ps[0:1, :], w3_sb[:, 1:2], h2_t[:, 1, :], start=False,
                             stop=True).then_inc(y_ps_done, 1)


def lay_out(inputs):
    f32 = np.float32
    k = np.asarray(inputs["L0_rec_kernel"])
    blocks = np.zeros((E, 2 * NU, 2, E), f32)
    for n in range(2 * NU):
        for h, (i, j) in enumerate(block_pairs(UNITS[n // 2], n % 2)):
            blocks[:, n, h, :] = k[:, pair_index(i, j), :]
    rows = lambda w, t: np.ascontiguousarray(w.reshape(t, P, -1).transpose(1, 0, 2))
    out = {
        "ids": np.ascontiguousarray(np.asarray(inputs["ids"]).reshape(BT, P, F).transpose(1, 2, 0)),
        "kblocks": blocks.reshape(E, 2 * NU * P),
        "dense_t": np.ascontiguousarray(np.asarray(inputs["dense_ctx"]).T),
        "w1": rows(np.asarray(inputs["W_top1"])[Z_ROWS], ZT),
        "b1": np.ascontiguousarray(np.asarray(inputs["b_top1"]).reshape(D1 // P, P).T),
        "w2": rows(np.asarray(inputs["W_top2"]), D1 // P),
        "b2": np.ascontiguousarray(np.asarray(inputs["b_top2"]).reshape(D2 // P, P).T),
        "w3": np.ascontiguousarray(np.asarray(inputs["W_top3"]).reshape(D2 // P, P).T),
        "ident": np.eye(P, dtype=f32),
        "sel": selectors(),
    }
    for f in range(F):
        out[f"tbl_{f}"] = np.ascontiguousarray(inputs[f"tbl_{f}"])
    return out


def kernel(**inputs):
    import concourse.bacc as bacc
    from concourse.bass_utils import run_bass_kernel_spmd

    arrays = lay_out(inputs)
    nc = bacc.Bacc("TRN2", target_bir_lowering=False, num_devices=1)
    ap = {name: nc.dram_tensor(name, a.shape, mybir.dt.from_np(a.dtype), kind="ExternalInput").ap()
          for name, a in arrays.items()}
    y = nc.dram_tensor("y", (1, B), F32, kind="ExternalOutput").ap()
    build(nc, ap["ids"], [ap[f"tbl_{f}"] for f in range(F)], ap["kblocks"], ap["dense_t"], ap["w1"],
          ap["b1"], ap["w2"], ap["b2"], ap["w3"], ap["ident"], ap["sel"], y)
    result = run_bass_kernel_spmd(nc, [arrays], core_ids=[0])
    return result.results[0]["y"].reshape(B, 1)
```

```python
from contextlib import ExitStack

import numpy as np

import concourse.bass as bass
from concourse import mybir

ALU = mybir.AluOpType
ACT = mybir.ActivationFunctionType
F32 = mybir.dt.float32
F32R = mybir.dt.float32r
I32 = mybir.dt.int32

B, F, E = 512, 32, 64
D1, D2, DENSE = 512, 256, 16
P = 128
BT = B // P
NC = F // 2
NPAIR = F * (F - 1) // 2
ZT = (NPAIR + DENSE) // P

CHUNK_UNITS = 4
CHUNK_BLOCKS = 2 * CHUNK_UNITS
CHUNK = CHUNK_BLOCKS * P
K_SLOTS = 3
SLOTS = 3
PROD_SLOTS = 6
SPLIT_SLOTS = 2
MOVE_SLOTS = 2
X_SLOTS = 6
SEL_AT = 31


def pair_index(i, j):
    return i * (2 * F - i - 1) // 2 + j - i - 1


def make_blocks():
    blocks = []
    for j in range(2, F):
        blocks += [(a, j) for a in range(j // 2)]
        if j % 4 == 3:
            blocks += [(j // 2 - 1, j - 2), (j // 2, j)]
    return [block for n in range(0, len(blocks), 2) for block in sorted(blocks[n:n + 2])]


def block_pairs(a, j):
    return [(i, j) for i in (2 * a, 2 * a + 1) if i < j]


def place_rows(blocks):
    room = [[32] * 4 for _ in range(ZT)]
    room[ZT - 1][3] -= DENSE
    tile, odd, places, rows = 0, None, [], np.full(NPAIR + DENSE, -1, np.int64)
    for a, j in blocks:
        pairs = block_pairs(a, j)
        if not any(room[tile]):
            tile += 1
        quad = int(np.argmax(room[tile])) if len(pairs) == 2 or odd is None else odd
        if len(pairs) == 1:
            odd = quad if odd is None else None
        full = 32 - (DENSE if (tile, quad) == (ZT - 1, 3) else 0)
        at = full - room[tile][quad]
        room[tile][quad] -= len(pairs)
        assert room[tile][quad] >= 0
        for k, (i, j) in enumerate(pairs):
            rows[tile * P + 32 * quad + at + k] = pair_index(i, j)
        places.append((tile, quad, at, at == 0, room[tile][quad] == 0))
    rows[rows < 0] = NPAIR + np.arange(DENSE)
    return places, rows


BLOCKS = make_blocks()
PLACES, Z_ROWS = place_rows(BLOCKS)
NU = len(BLOCKS) // 2
N_CHUNKS = NU // CHUNK_UNITS
Z_CLOSES = [max(n for n, p in enumerate(PLACES) if p[0] == t) for t in range(ZT)]
Z_SIGNALS = sorted(set(Z_CLOSES) | set(range(3, 2 * NU, 4)))
Z_ROWS_LAST = P - DENSE

TURNED = range(1, 18)
MOVED = range(TURNED.stop // 2, NC)


def z_signal(block):
    return 1 + sum(n < block for n in Z_SIGNALS)


POOL_HELPS, POOL_EVERY = 90.0, 2


def make_steps():
    lat, row, arrival = 0.2, 1.06, 2.0
    unit_t, sum_t, turn_t, mult_t, klo_t, khi_t, pool_t = 0.88, 1.0, 0.43, 1.2, 1.15, 1.05, 2.4
    pe = act = dve = 0.0
    pool = 3.5
    steps, on_pool = [], []
    arrive, split_end, hl_turned, xt_out, xt_turned, klo_end = [], [], [], [], [], []
    unit_end, mult_end, sums_end, slot_free = [], [], [], []
    x_ready = {}

    def gather():
        nonlocal pool
        f = len(arrive)
        if f % 2 == 0 and f // 2 >= X_SLOTS:
            pool = max(pool, xt_turned[f // 2 - X_SLOTS])
        pool += row * BT
        arrive.append(pool + arrival)
        steps.append(("gather", f))

    def can_gather():
        c = len(arrive) // 2
        return len(arrive) < F and (c < X_SLOTS or c - X_SLOTS < len(xt_turned))

    def ksplit(m):
        nonlocal act, dve, pool
        free = unit_end[CHUNK_UNITS * (m - K_SLOTS + 1) - 1] if m >= K_SLOTS else 0.0
        act = max(act, free + lat, 6.0 + 3 * m) + khi_t
        if len(arrive) == F or (act > POOL_HELPS and m % POOL_EVERY == 0):
            pool = max(pool, act + lat) + pool_t
            klo_end.append(pool)
            on_pool.append(m)
        else:
            dve = max(dve, act + lat) + klo_t
            klo_end.append(dve)
        steps.append(("ksplit", m))

    def slot():
        return slot_free[-SLOTS] + lat if len(slot_free) >= SLOTS else 0.0

    for m in range(K_SLOTS):
        ksplit(m)
    while len(sums_end) < NU // 2 - 1:
        options = []
        f, c, u, v = len(hl_turned) + 1, len(xt_out), len(unit_end), len(sums_end)
        if f <= len(split_end):
            options.append((max(pe, split_end[f - 1] + lat, slot()), 0, "hl"))
        if c < NC and 2 * c + 1 < len(arrive):
            at = max(arrive[2 * c + 1], xt_out[-1] + lat if c else 0.0)
            options.append((max(pe, at), 1, "xt"))
        if u < NU:
            pair = BLOCKS[2 * u:2 * u + 2]
            enough = u < PROD_SLOTS or len(sums_end) > (u - PROD_SLOTS) // 2
            if all(j in x_ready for _, j in pair) and max(a for a, _ in pair) < c and enough:
                at = max(x_ready[j] for _, j in pair) + lat
                options.append((max(pe, at, slot(), klo_end[u // CHUNK_UNITS] + lat), 2, "unit"))
        if 2 * v + 2 <= u and v < NU // 2 - 1:
            options.append((max(pe, mult_end[2 * v + 1] + lat), 3, "sum"))
        soon = min(options)[0] if options else 1e9
        if can_gather() and pool < soon + 1.0:
            gather()
            continue
        f = len(split_end) + 1
        if f in TURNED and f < len(arrive) and arrive[f] <= soon and f - 1 - SPLIT_SLOTS < len(hl_turned):
            free = hl_turned[f - 1 - SPLIT_SLOTS] if f > SPLIT_SLOTS else 0.0
            act = max(act, arrive[f], free + lat) + 0.41
            dve = max(dve, act + lat) + 0.37
            split_end.append(dve)
            steps.append(("split", f))
            continue
        at, _, what = min(options)
        if what == "hl":
            f = len(hl_turned) + 1
            pe = at + turn_t
            hl_turned.append(pe)
            act = max(act, pe + lat) + 0.58
            x_ready[f] = act
            slot_free.append(act)
            steps.append(("hl", f))
        if what == "xt":
            pe = at + turn_t
            act = max(act, pe + lat) + 0.58
            xt_turned.append(pe)
            xt_out.append(act)
            steps.append(("xt", c))
            if c in MOVED:
                act += lat + 0.6
                dve = max(dve, act + lat) + 0.65
                x_ready[2 * c] = x_ready[2 * c + 1] = dve + 3.0
                steps.append(("move", c))
        if what == "unit":
            pe = at + unit_t
            unit_end.append(pe)
            dve = max(dve, pe + lat, xt_out[max(a for a, _ in pair)] + lat) + mult_t
            mult_end.append(dve)
            slot_free.append(dve)
            steps.append(("unit", u))
            m = (u + 1) // CHUNK_UNITS + K_SLOTS - 1
            if (u + 1) % CHUNK_UNITS == 0 and m < N_CHUNKS:
                ksplit(m)
        if what == "sum":
            pe = at + sum_t
            sums_end.append(pe)
            steps.append(("sum", v))
            if any(4 * v <= z < 4 * v + 4 for z in Z_CLOSES[:ZT - 2]):
                act = max(act, pe + lat) + 0.6
                pe = max(pe, act + lat)

    return steps, on_pool


STEPS, POOL_CHUNKS = make_steps()
SLOT_USERS = [step for step in STEPS if step[0] in ("hl", "unit")]
SLOT_OF = {step: n % SLOTS for n, step in enumerate(SLOT_USERS)}
LAST_SLOT = SLOT_OF["unit", NU - 1]
TOWER_SLOTS = [(LAST_SLOT + 1) % SLOTS, (LAST_SLOT + 2) % SLOTS]
TURN_BANK_TILE = ZT - 1


def selectors():
    s = np.zeros((P, 2, 64), np.float32)
    s[:E, :, SEL_AT] = 1
    s[E:, 0, SEL_AT + 1] = 1
    return s


def build(nc, ids, tables, kblocks, dense_t, w1, b1, w2, b2, w3, ident, sel, y):
    with ExitStack() as ctx:
        def sb(name, shape, dt=F32):
            return ctx.enter_context(nc.sbuf_tensor(name, shape, dt))

        def sem(name):
            return ctx.enter_context(nc.semaphore(name))

        ids_sb = sb("ids_sb", [P, F, BT], I32)
        ident_sb = sb("ident_sb", [P, P])
        sel_sb = sb("sel_sb", [P, 2, 64])
        x_nat = sb("x_nat", [P, X_SLOTS, BT, 2, E])
        x_parts = sb("x_parts", [P, SPLIT_SLOTS, BT, 2, E], F32R)
        x_t = sb("x_t", [P, NC, B])
        x_hl = sb("x_hl", [P, F, B], F32R)
        move_hi = sb("move_hi", [P, MOVE_SLOTS, B], F32R)
        move_lo = sb("move_lo", [P, MOVE_SLOTS, B], F32R)
        k_raw = sb("k_raw", [P, K_SLOTS, CHUNK])
        k_hi = sb("k_hi", [P, K_SLOTS, CHUNK], F32R)
        k_lo = sb("k_lo", [P, K_SLOTS, CHUNK], F32R)
        prod = sb("prod", [P, PROD_SLOTS, 2, B])
        z_t = sb("z_t", [P, ZT, B])
        w1_sb = sb("w1_sb", [P, ZT, D1])
        w2_sb = sb("w2_sb", [P, D1 // P, D2])
        w3_sb = sb("w3_sb", [P, D2 // P])
        b1_sb = sb("b1_sb", [P, D1 // P])
        b2_sb = sb("b2_sb", [P, D2 // P])
        h1_t = k_raw[:, 0:2, :].rearrange("p s (n b) -> p (s n) b", b=B)
        h2_t = k_raw[:, 2, :].rearrange("p (n b) -> p n b", b=B)
        y_sb = sb("y_sb", [1, B])

        t_ps = ctx.enter_context(nc.psum_tensor("t_ps", [P, 2 * SLOTS, B], F32))
        z_ps = ctx.enter_context(nc.psum_tensor("z_ps", [P, B], F32))
        turn_ps = ctx.enter_context(nc.psum_tensor("turn_ps", [P, BT, P], F32))

        def h1_ps(n):
            return t_ps[:, 2 * TOWER_SLOTS[n // 2] + n % 2, :]

        def h2_ps(n):
            return t_ps[:, 2 * LAST_SLOT + n, :]

        ids_in = sem("ids_in")
        consts_in = sem("consts_in")
        tower_in = sem("tower_in")
        dense_in = sem("dense_in")
        gathered = [sem(f"gathered{f}") for f in range(F)]
        k_in = [sem(f"k_in{s}") for s in range(K_SLOTS)]
        x_hi_done = sem("x_hi_done")
        x_lo_done = sem("x_lo_done")
        hl_turned = sem("hl_turned")
        hl_out = sem("hl_out")
        xt_turned = sem("xt_turned")
        xt_out = sem("xt_out")
        move_hi_done = sem("move_hi_done")
        move_lo_done = sem("move_lo_done")
        moved = [sem(f"moved{s}") for s in range(MOVE_SLOTS)]
        k_hi_done = sem("k_hi_done")
        k_lo_dve = sem("k_lo_dve")
        k_lo_pool = sem("k_lo_pool")
        units_done = sem("units_done")
        prod_done = sem("prod_done")
        z_summed = sem("z_summed")
        z_out = sem("z_out")
        h1_ps_done = sem("h1_ps_done")
        h1_act = sem("h1_act")
        h1_dve = sem("h1_dve")
        h2_ps_done = sem("h2_ps_done")
        h2_act = sem("h2_act")
        h2_dve = sem("h2_dve")
        y_ps_done = sem("y_ps_done")
        y_done = sem("y_done")
        y_stored = sem("y_stored")

        block = ctx.enter_context(nc.Block())

        def wait_k_lo(eng, m):
            if m in POOL_CHUNKS:
                eng.wait_ge(k_lo_pool, POOL_CHUNKS.index(m) + 1)
            else:
                eng.wait_ge(k_lo_dve, m + 1 - sum(k < m for k in POOL_CHUNKS))

        def wait_moved(eng, c):
            k = MOVED.index(c)
            eng.wait_ge(moved[k % MOVE_SLOTS], 64 * (k // MOVE_SLOTS + 1))

        def z_bank(t):
            if t == TURN_BANK_TILE:
                return turn_ps[:, :, :].rearrange("p t b -> p (t b)")
            return z_ps[:, :]

        @block.sync
        def _(sp):
            sp.dma_start(ids_sb[:, :, :], ids).then_inc(ids_in, 16)
            sp.dma_start(ident_sb[:, :], ident).then_inc(consts_in, 16)
            sp.dma_start(sel_sb[:, :, :], sel).then_inc(consts_in, 16)

            def load_k(m):
                s = m % K_SLOTS
                if m >= K_SLOTS:
                    wait_k_lo(sp, m - K_SLOTS)
                for half in range(2):
                    sp.dma_start(k_raw[half * E:(half + 1) * E, s, :],
                                 kblocks[:, m * CHUNK:(m + 1) * CHUNK]).then_inc(k_in[s], 16)

            def load_tower():
                sp.dma_start(w1_sb[:, :, :], w1).then_inc(tower_in, 16)
                sp.dma_start(w2_sb[:, :, :], w2).then_inc(tower_in, 16)
                sp.dma_start(w3_sb[:, :], w3).then_inc(tower_in, 16)
                sp.dma_start(b1_sb[:, :], b1).then_inc(tower_in, 16)
                sp.dma_start(b2_sb[:, :], b2).then_inc(tower_in, 16)
                sp.dma_start(z_t[P - DENSE:P, ZT - 1, :], dense_t).then_inc(dense_in, 16)

            for m in range(K_SLOTS):
                load_k(m)
            for what, n in STEPS:
                if what == "ksplit" and n + K_SLOTS < N_CHUNKS:
                    load_k(n + K_SLOTS)
                if what == "ksplit" and n == 2 * K_SLOTS:
                    load_tower()
                if what == "move":
                    s = MOVED.index(n) % MOVE_SLOTS
                    sp.wait_ge(move_lo_done, MOVED.index(n) + 1)
                    for parity in range(2):
                        src = slice(parity * E, (parity + 1) * E)
                        for dst, part in ((slice(0, E), move_hi), (slice(E, P), move_lo)):
                            sp.dma_start(x_hl[dst, 2 * n + parity, :].bitcast(F32),
                                         part[src, s, :].bitcast(F32)).then_inc(moved[s], 16)
            sp.wait_ge(y_done, 1)
            sp.dma_start(y, y_sb[:, :]).then_inc(y_stored, 16)
            sp.wait_ge(y_stored, 16)

        @block.gpsimd
        def _(pool):
            pool.wait_ge(ids_in, 16)
            for what, n in STEPS:
                if what == "gather":
                    f, c = n, n // 2
                    if f % 2 == 0 and c >= X_SLOTS:
                        pool.wait_ge(xt_turned, c - X_SLOTS + 1)
                        if 2 * (c - X_SLOTS) + 1 in TURNED:
                            pool.wait_ge(x_lo_done, 2 * (c - X_SLOTS) + 1)
                    for bt in range(BT):
                        pool.indirect_dma_start(
                            x_nat[:, c % X_SLOTS, bt, f % 2, :], None, tables[f],
                            bass.IndirectOffsetOnAxis(ap=ids_sb[:, f, bt:bt + 1], axis=0),
                        ).then_inc(gathered[f], 16)
                if what == "ksplit" and n in POOL_CHUNKS:
                    s = n % K_SLOTS
                    pool.wait_ge(k_hi_done, n + 1)
                    pool.wait_ge(units_done, CHUNK_UNITS * (n - K_SLOTS + 1))
                    nc.gpsimd.tensor_tensor(k_lo[:, s, :], k_raw[:, s, :], k_hi[:, s, :].bitcast(F32),
                                            ALU.subtract).then_inc(k_lo_pool, 1)

        @block.scalar
        def _(act):
            for what, n in STEPS:
                if what == "ksplit":
                    s = n % K_SLOTS
                    act.wait_ge(k_in[s], 32 * (n // K_SLOTS + 1))
                    if n >= K_SLOTS:
                        act.wait_ge(units_done, CHUNK_UNITS * (n - K_SLOTS + 1))
                    nc.scalar.activation(k_hi[:, s, :], k_raw[:, s, :], ACT.Copy).then_inc(k_hi_done, 1)
                if what == "split":
                    act.wait_ge(gathered[n], 16 * BT)
                    if n > SPLIT_SLOTS:
                        act.wait_ge(hl_turned, n - SPLIT_SLOTS)
                    nc.scalar.activation(x_parts[:, n % SPLIT_SLOTS, :, 0, :],
                                         x_nat[:, (n // 2) % X_SLOTS, :, n % 2, :],
                                         ACT.Copy).then_inc(x_hi_done, 1)
                if what == "hl":
                    act.wait_ge(hl_turned, n)
                    nc.scalar.activation(x_hl[:, n, :], t_ps[:, 2 * SLOT_OF[what, n], :],
                                         ACT.Copy).then_inc(hl_out, 1)
                if what == "xt":
                    act.wait_ge(xt_turned, n + 1)
                    nc.scalar.activation(x_t[:, n, :], turn_ps[:, :, :].rearrange("p t b -> p (t b)"),
                                         ACT.Copy).then_inc(xt_out, 1)
                if what == "move":
                    act.wait_ge(xt_out, n + 1)
                    if n - MOVE_SLOTS in MOVED:
                        wait_moved(act, n - MOVE_SLOTS)
                    nc.scalar.activation(move_hi[:, MOVED.index(n) % MOVE_SLOTS, :], x_t[:, n, :],
                                         ACT.Copy).then_inc(move_hi_done, 1)
                if what == "sum":
                    for t in range(ZT - 1):
                        if 4 * n <= Z_CLOSES[t] < 4 * n + 4:
                            act.wait_ge(z_summed, z_signal(Z_CLOSES[t]))
                            nc.scalar.activation(z_t[:, t, :], z_bank(t), ACT.Copy).then_inc(z_out, 1)

            act.wait_ge(z_summed, z_signal(Z_CLOSES[ZT - 1]))
            nc.scalar.activation(z_t[0:Z_ROWS_LAST, ZT - 1, :], z_bank(ZT - 1)[0:Z_ROWS_LAST, :],
                                 ACT.Copy).then_inc(z_out, 1)
            for n in range(0, D1 // P, 2):
                act.wait_ge(h1_ps_done, n + 1)
                act.wait_ge(tower_in, 16 * 5)
                nc.scalar.activation(h1_t[:, n, :], h1_ps(n), ACT.Relu,
                                     bias=b1_sb[:, n:n + 1]).then_inc(h1_act, 1)
            act.wait_ge(h2_ps_done, 1)
            nc.scalar.activation(h2_t[:, 0, :], h2_ps(0), ACT.Relu,
                                 bias=b2_sb[:, 0:1]).then_inc(h2_act, 1)

        @block.vector
        def _(dve):
            for what, n in STEPS:
                if what == "split":
                    dve.wait_ge(x_hi_done, n)
                    parts = x_parts[:, n % SPLIT_SLOTS, :, :, :]
                    nc.vector.tensor_tensor(parts[:, :, 1, :], x_nat[:, (n // 2) % X_SLOTS, :, n % 2, :],
                                            parts[:, :, 0, :].bitcast(F32),
                                            ALU.subtract).then_inc(x_lo_done, 1)
                if what == "move":
                    s = MOVED.index(n) % MOVE_SLOTS
                    dve.wait_ge(move_hi_done, MOVED.index(n) + 1)
                    nc.vector.tensor_tensor(move_lo[:, s, :], x_t[:, n, :], move_hi[:, s, :].bitcast(F32),
                                            ALU.subtract).then_inc(move_lo_done, 1)
                if what == "ksplit" and n not in POOL_CHUNKS:
                    s = n % K_SLOTS
                    dve.wait_ge(k_hi_done, n + 1)
                    if n >= K_SLOTS:
                        dve.wait_ge(units_done, CHUNK_UNITS * (n - K_SLOTS + 1))
                    nc.vector.tensor_tensor(k_lo[:, s, :], k_raw[:, s, :], k_hi[:, s, :].bitcast(F32),
                                            ALU.subtract).then_inc(k_lo_dve, 1)
                if what == "unit":
                    s, a, a2 = SLOT_OF[what, n], BLOCKS[2 * n][0], BLOCKS[2 * n + 1][0]
                    if a == a2:
                        by = x_t[:, a:a + 1, :].to_broadcast([P, 2, B])
                    else:
                        by = x_t[:, a:a2 + 1:a2 - a, :]
                    dve.wait_ge(units_done, n + 1)
                    dve.wait_ge(xt_out, max(a, a2) + 1)
                    if n >= PROD_SLOTS:
                        dve.wait_ge(z_summed, z_signal(2 * (n - PROD_SLOTS) + 1))
                    nc.vector.tensor_tensor(prod[:, n % PROD_SLOTS, :, :], t_ps[:, 2 * s:2 * s + 2, :],
                                            by, ALU.mult).then_inc(prod_done, 1)
            for k, n in enumerate(range(1, D1 // P, 2)):
                dve.wait_ge(h1_ps_done, n + 1)
                dve.wait_ge(tower_in, 16 * 5)
                nc.vector.tensor_scalar(h1_t[:, n, :], h1_ps(n), b1_sb[:, n:n + 1], 0.0,
                                        ALU.add, ALU.max).then_inc(h1_dve, 1)
            dve.wait_ge(h2_ps_done, 2)
            nc.vector.tensor_scalar(h2_t[:, 1, :], h2_ps(1), b2_sb[:, 1:2], 0.0,
                                    ALU.add, ALU.max).then_inc(h2_dve, 1)
            dve.wait_ge(y_ps_done, 1)
            nc.vector.tensor_copy(y_sb[:, :], z_ps[0:1, :]).then_inc(y_done, 1)

        @block.tensor
        def _(pe):
            def wait_slot(step):
                use = SLOT_USERS.index(step)
                if use >= SLOTS:
                    what, n = SLOT_USERS[use - SLOTS]
                    if what == "hl":
                        pe.wait_ge(hl_out, n)
                    else:
                        pe.wait_ge(prod_done, n + 1)
                return SLOT_OF[step]

            def turn_hl(f):
                s = wait_slot(("hl", f))
                pe.wait_ge(x_lo_done, f)
                for bt in range(BT):
                    part = x_parts[:, f % SPLIT_SLOTS, bt, :, :].bitcast(F32)
                    last = nc.tensor.transpose(t_ps[:, 2 * s, bt * P:(bt + 1) * P],
                                               part.rearrange("p h e -> p (h e)"), ident_sb[:, :])
                last.then_inc(hl_turned, 1)

            def turn_xt(c):
                for f in (2 * c, 2 * c + 1):
                    pe.wait_ge(gathered[f], 16 * BT)
                if c:
                    pe.wait_ge(xt_out, c)
                for bt in range(BT):
                    last = nc.tensor.transpose(turn_ps[:, bt, :],
                                               x_nat[:, c % X_SLOTS, bt, :, :].rearrange("p a e -> p (a e)"),
                                               ident_sb[:, :])
                last.then_inc(xt_turned, 1)

            def products(u):
                s = wait_slot(("unit", u))
                m = u // CHUNK_UNITS
                if u % CHUNK_UNITS == 0:
                    wait_k_lo(pe, m)
                for q in range(2):
                    at = ((2 * u + q) % CHUNK_BLOCKS) * P
                    j = BLOCKS[2 * u + q][1]
                    if j in TURNED:
                        pe.wait_ge(hl_out, j)
                    else:
                        wait_moved(pe, j // 2)
                    for k, part in enumerate((k_hi, k_lo)):
                        last = nc.tensor.matmul(t_ps[:, 2 * s + q, :], part[:, m % K_SLOTS, at:at + P],
                                                x_hl[:, j, :], start=(k == 0), stop=(k == 1))
                last.then_inc(units_done, 1)

            def sums(v):
                pe.wait_ge(prod_done, 2 * v + 2)
                for n in range(4 * v, 4 * v + 4):
                    tile, quad, at, first, final = PLACES[n]
                    lone = int(len(block_pairs(*BLOCKS[n])) == 1)
                    if tile == TURN_BANK_TILE and n == Z_CLOSES[tile - 1] + 1:
                        pe.wait_ge(xt_out, NC)
                    elif tile and n == Z_CLOSES[tile - 1] + 1:
                        pe.wait_ge(z_out, tile)
                    last = nc.tensor.matmul(z_bank(tile)[32 * quad:32 * quad + 32, :],
                                            sel_sb[:, lone, SEL_AT - at:SEL_AT - at + 32],
                                            prod[:, (n // 2) % PROD_SLOTS, n % 2, :],
                                            start=first, stop=final)
                    if n in Z_SIGNALS:
                        last.then_inc(z_summed, 1)

            def tower1(t):
                pe.wait_ge(z_out, t + 1)
                for n in range(D1 // P):
                    last = nc.tensor.matmul(h1_ps(n), w1_sb[:, t, n * P:(n + 1) * P], z_t[:, t, :],
                                            start=(t == 0), stop=(t == ZT - 1))
                    if t == ZT - 1:
                        last.then_inc(h1_ps_done, 1)

            pe.wait_ge(consts_in, 32)
            for what, n in STEPS:
                if what == "hl":
                    turn_hl(n)
                if what == "xt":
                    turn_xt(n)
                if what == "unit":
                    products(n)
                if what == "sum":
                    sums(n)
            pe.wait_ge(tower_in, 16 * 5)
            pe.wait_ge(dense_in, 16)
            pe.wait_ge(prod_done, NU - 1)
            for t in range(ZT - 1):
                tower1(t)
            sums(NU // 2 - 1)
            tower1(ZT - 1)
            for t in range(D1 // P):
                if t % 2 == 0:
                    pe.wait_ge(h1_act, t // 2 + 1)
                else:
                    pe.wait_ge(h1_dve, t // 2 + 1)
                for n in range(D2 // P):
                    last = nc.tensor.matmul(h2_ps(n), w2_sb[:, t, n * P:(n + 1) * P],
                                            h1_t[:, t, :], start=(t == 0), stop=(t == D1 // P - 1))
                    if t == D1 // P - 1:
                        last.then_inc(h2_ps_done, 1)
            pe.wait_ge(h2_act, 1)
            nc.tensor.matmul(z_ps[0:1, :], w3_sb[:, 0:1], h2_t[:, 0, :], start=True, stop=False)
            pe.wait_ge(h2_dve, 1)
            nc.tensor.matmul(z_ps[0:1, :], w3_sb[:, 1:2], h2_t[:, 1, :], start=False,
                             stop=True).then_inc(y_ps_done, 1)


def lay_out(inputs):
    f32 = np.float32
    k = np.asarray(inputs["L0_rec_kernel"])
    blocks = np.zeros((E, 2 * NU, 2, E), f32)
    for n in range(2 * NU):
        for h, (i, j) in enumerate(block_pairs(*BLOCKS[n])):
            blocks[:, n, h, :] = k[:, pair_index(i, j), :]
    rows = lambda w, t: np.ascontiguousarray(w.reshape(t, P, -1).transpose(1, 0, 2))
    out = {
        "ids": np.ascontiguousarray(np.asarray(inputs["ids"]).reshape(BT, P, F).transpose(1, 2, 0)),
        "kblocks": blocks.reshape(E, 2 * NU * P),
        "dense_t": np.ascontiguousarray(np.asarray(inputs["dense_ctx"]).T),
        "w1": rows(np.asarray(inputs["W_top1"])[Z_ROWS], ZT),
        "b1": np.ascontiguousarray(np.asarray(inputs["b_top1"]).reshape(D1 // P, P).T),
        "w2": rows(np.asarray(inputs["W_top2"]), D1 // P),
        "b2": np.ascontiguousarray(np.asarray(inputs["b_top2"]).reshape(D2 // P, P).T),
        "w3": np.ascontiguousarray(np.asarray(inputs["W_top3"]).reshape(D2 // P, P).T),
        "ident": np.eye(P, dtype=f32),
        "sel": selectors(),
    }
    for f in range(F):
        out[f"tbl_{f}"] = np.ascontiguousarray(inputs[f"tbl_{f}"])
    return out


def kernel(**inputs):
    import concourse.bacc as bacc
    from concourse.bass_utils import run_bass_kernel_spmd

    arrays = lay_out(inputs)
    nc = bacc.Bacc("TRN2", target_bir_lowering=False, num_devices=1)
    ap = {name: nc.dram_tensor(name, a.shape, mybir.dt.from_np(a.dtype), kind="ExternalInput").ap()
          for name, a in arrays.items()}
    y = nc.dram_tensor("y", (1, B), F32, kind="ExternalOutput").ap()
    build(nc, ap["ids"], [ap[f"tbl_{f}"] for f in range(F)], ap["kblocks"], ap["dense_t"], ap["w1"],
          ap["b1"], ap["w2"], ap["b2"], ap["w3"], ap["ident"], ap["sel"], y)
    result = run_bass_kernel_spmd(nc, [arrays], core_ids=[0])
    return result.results[0]["y"].reshape(B, 1)
```
